# Optimizing a Trainium2 kernel written in Bass

```python
import numpy as np
import jax
import jax.numpy as jnp

def _softmax(x, axis=-1):
    return jax.nn.softmax(x, axis=axis)

def _gelu(x):
    return jax.nn.gelu(x, approximate=True)

def _silu(x):
    return jax.nn.silu(x)

def _sigmoid(x):
    return jax.nn.sigmoid(x)

def _layernorm(x, axis=-1, eps=1e-05):
    m = jnp.mean(x, axis=axis, keepdims=True)
    v = jnp.var(x, axis=axis, keepdims=True)
    return (x - m) / jnp.sqrt(v + eps)

def _scatter_add(tgt, idx, src, axis=0):
    return tgt.at[idx].add(src)

def _segment_sum(src, seg, n):
    return jax.ops.segment_sum(src, seg, n)
kernel_name = 'mk_cond_resid_d1_seqx_r4_a0b8fd'

def setup_inputs(seed: int=0):
    np.random.seed(seed)
    _w = jnp.asarray

    def _rec_inputs():
        import jax
        import jax.numpy as jnp
        _rk = jax.random.key(seed)
        x = -0.000125 + 0.9999 * jax.random.normal(jax.random.fold_in(_rk, 1), (32, 256, 256), jnp.float32)
        _lenS = 256 - jax.random.randint(jax.random.fold_in(_rk, 7), (32,), 0, max(1, 256 // 4) + 1, jnp.int32)
        _lenS2 = 256 - jax.random.randint(jax.random.fold_in(_rk, 8), (32,), 0, max(1, 256 // 4) + 1, jnp.int32)
        cond_1024 = -0.00493535 + 1.00056 * jax.random.normal(jax.random.fold_in(_rk, 11), (32, 256), jnp.float32)
        return (x, cond_1024)
    x, cond_1024 = _rec_inputs()

    def _L0_cond_setup():
        import jax, jax.numpy as jnp
        import numpy as np
        import math
        N, T, D, H = (64, 128, 256, 256)
        key = jax.random.key(seed)
        k1, k2, k3, k4 = jax.random.split(key, 4)
        x = jax.random.normal(k1, (N, T, D), dtype=jnp.float32)
        h0 = jax.random.normal(k2, (N, H), dtype=jnp.float32)
        Wx = jax.random.normal(k3, (D, 4 * H), dtype=jnp.float32) / math.sqrt(D)
        Wh = jax.random.normal(k4, (H, 4 * H), dtype=jnp.float32) / math.sqrt(H)
        b = jnp.zeros((4 * H,), dtype=jnp.float32)
        return {'x': x, 'h0': h0, 'Wx': Wx, 'Wh': Wh, 'b': b}
    _L0_cond_all = _L0_cond_setup()
    _L0_cond_in = {k: v for k, v in _L0_cond_all.items() if k in ('Wx', 'Wh', 'b')}
    del _L0_cond_all
    return {'x': x, 'cond_1024': cond_1024, 'L0_cond_Wx': _L0_cond_in['Wx'], 'L0_cond_Wh': _L0_cond_in['Wh'], 'L0_cond_b': _L0_cond_in['b']}

def reference(x, cond_1024, L0_cond_Wx, L0_cond_Wh, L0_cond_b):
    import jax
    import jax.numpy as jnp

    def _L0_cond_ref(x, h0, Wx, Wh, b):
        import jax, jax.numpy as jnp
        import numpy as np
        import math
        N, T, D, H = (64, 128, 256, 256)
        Hdim = h0.shape[1]
        xW = jnp.einsum('ntd,dg->ntg', x, Wx) + b

        def step(carry, xw_t):
            prev_h, prev_c = carry
            a = xw_t + prev_h @ Wh
            i = jax.nn.sigmoid(a[:, :Hdim])
            f = jax.nn.sigmoid(a[:, Hdim:2 * Hdim])
            o = jax.nn.sigmoid(a[:, 2 * Hdim:3 * Hdim])
            g = jnp.tanh(a[:, 3 * Hdim:])
            next_c = f * prev_c + i * g
            next_h = o * jnp.tanh(next_c)
            return ((next_h, next_c), next_h)
        c0 = jnp.zeros_like(h0)
        _, hs = jax.lax.scan(step, (h0, c0), jnp.swapaxes(xW, 0, 1))
        return jnp.swapaxes(hs, 0, 1)
    x = x + _L0_cond_ref(x, cond_1024, L0_cond_Wx, L0_cond_Wh, L0_cond_b)
    return x

_drawn_inputs = setup_inputs


def setup_inputs(seed=0):
    import zlib

    import numpy as np

    out = dict(_drawn_inputs(seed))
    spreads = {'L0_cond_b': (0.0, 0.1)}
    factors = {'cond_1024': 4.679}
    for name, (base, spread) in spreads.items():
        noise = np.random.default_rng([zlib.crc32(name.encode()), seed]).standard_normal(out[name].shape)
        drawn = base * np.exp(spread * noise) if base else spread * noise
        out[name] = jnp.asarray(drawn.astype(out[name].dtype))
    for name, factor in factors.items():
        out[name] = (out[name] * factor).astype(out[name].dtype)
    return out
```

```python
from contextlib import ExitStack

import concourse.bass as bass
from concourse import mybir

F32 = mybir.dt.float32
BF16 = mybir.dt.bfloat16
ACT = mybir.ActivationFunctionType
ALU = mybir.AluOpType

P = 128
B, T, D = 32, 256, 256
H = 256
GATES = 4
QUADS = P // B
HS = H // QUADS
BLOCKS = HS // 32
CHUNK = 8
SLOTS = 2
ROUND = CHUNK * SLOTS
TURNS = T // ROUND
DMA = 16 * QUADS

GATE_I, GATE_F, GATE_O, GATE_G = range(GATES)
GROUPS = ((GATE_I, 2), (GATE_G, 1), (GATE_O, 1))


def lstm_residual(nc, x, cond, Wx, Wh, bias, out):
    ctx = ExitStack()
    with ctx:
        def sb(name, shape, dt=F32):
            return ctx.enter_context(nc.sbuf_tensor(name, shape, dt))

        def sem(name):
            return ctx.enter_context(nc.semaphore(name))

        wx_sb = sb("wx_sb", [P, BLOCKS, GATES, H])
        wh_sb = sb("wh_sb", [P, BLOCKS, GATES, H])
        bias_f32 = sb("bias_f32", [P, GATES, HS])
        bias_rest = sb("bias_rest", [P, GATES, HS])
        bias_hi = sb("bias_hi", [P, GATES, HS], BF16)
        bias_mid = sb("bias_mid", [P, GATES, HS], BF16)
        bias_lo = sb("bias_lo", [P, GATES, HS], BF16)
        bias_parts = sb("bias_parts", [P, GATES, HS], BF16)
        spread = sb("spread", [P, P], BF16)
        x_sb = sb("x_sb", [P, SLOTS, CHUNK, HS])
        y_sb = sb("y_sb", [P, SLOTS, CHUNK, HS])
        cond_sb = sb("cond_sb", [P, HS])
        xT = sb("xT", [P, 2, HS])
        hT = sb("hT", [P, HS])
        h = sb("h", [P, 2, HS])
        c = sb("c", [P, HS])
        sig_if = sb("sig_if", [P, 2, HS])
        tanh_g = sb("tanh_g", [P, HS])
        sig_o = sb("sig_o", [P, HS])
        tanh_c = sb("tanh_c", [P, HS])
        fc = sb("fc", [P, HS])
        ig = sb("ig", [P, HS])

        gates = [[ctx.enter_context(nc.psum_tensor(f"gates{g}_{p}", [P, 512], F32))
                  for p in range(2)] for g in range(len(GROUPS))]

        s_wx = sem("wx_loaded")
        s_wh = sem("wh_loaded")
        s_bias = sem("bias_loaded")
        s_cond = sem("cond_loaded")
        s_x = [sem(f"x_loaded{s}") for s in range(SLOTS)]
        s_stored = [sem(f"y_stored{s}") for s in range(SLOTS)]
        s_zero = sem("zeros_written")
        s_split = sem("bias_split_steps")
        s_spread = sem("spread_ready")
        s_parts = sem("bias_parts_ready")
        s_xT = sem("xT_ready")
        s_hT = sem("hT_ready")
        s_if = sem("if_in_psum")
        s_g = sem("g_in_psum")
        s_o = sem("o_in_psum")
        s_sig_if = sem("sig_if_ready")
        s_tanh_g = sem("tanh_g_ready")
        s_sig_o = sem("sig_o_ready")
        s_tanh_c = sem("tanh_c_ready")
        s_fc = sem("fc_ready")
        s_ig = sem("ig_ready")
        s_c = sem("c_ready")
        s_h = sem("h_ready")
        s_y = sem("y_ready")

        block = ctx.enter_context(nc.Block())

        def quad(q):
            return slice(B * q, B * q + B)

        def hid(q):
            return slice(HS * q, HS * q + HS)

        @block.sync
        def _(sp):
            def load_x(t0, slot):
                for q in range(QUADS):
                    sp.dma_start(x_sb[quad(q), slot], x[:, bass.ds(t0, CHUNK), hid(q)]).then_inc(s_x[slot], 16)

            def store_y(t0, slot):
                for q in range(QUADS):
                    sp.dma_start(out[:, bass.ds(t0, CHUNK), hid(q)], y_sb[quad(q), slot]).then_inc(s_stored[slot], 16)

            load_x(0, 0)
            for q in range(QUADS):
                sp.dma_start(cond_sb[quad(q), :], cond[:, hid(q)]).then_inc(s_cond, 16)
            for q in range(QUADS):
                sp.dma_start(wh_sb[quad(q)].rearrange("r k g c -> r k (g c)"),
                             Wh[hid(q), :].rearrange("(k r) n -> r k n", k=BLOCKS)).then_inc(s_wh, 16)
            load_x(CHUNK, 1)
            with sp.Fori(0, TURNS - 1) as turn:
                t0 = turn * ROUND
                for slot in range(SLOTS):
                    sp.wait_ge(s_y, t0 + CHUNK * (slot + 1))
                    store_y(t0 + CHUNK * slot, slot)
                    load_x(t0 + CHUNK * slot + ROUND, slot)
            for slot in range(SLOTS):
                sp.wait_ge(s_y, T - ROUND + CHUNK * (slot + 1))
                store_y(T - ROUND + CHUNK * slot, slot)
            for slot in range(SLOTS):
                sp.wait_ge(s_stored[slot], DMA * (T // ROUND))

        @block.gpsimd
        def _(pool):
            nc.gpsimd.memset(spread[:, :], 1.0).then_inc(s_zero, 1)
            pool.wait_ge(s_zero, 1)
            for part in range(QUADS):
                rows = spread[quad(part), :]
                nc.gpsimd.affine_select(out=rows, in_=rows, compare_op=ALU.is_ge, fill=0.0, base=0,
                                        pattern=[[1, P]], channel_multiplier=-B).then_inc(s_zero, 1)
                pool.wait_ge(s_zero, 2 * part + 2)
                nc.gpsimd.affine_select(out=rows, in_=rows, compare_op=ALU.is_ge, fill=0.0, base=B - 1,
                                        pattern=[[-1, P]], channel_multiplier=B).then_inc(s_zero, 1)
                pool.wait_ge(s_zero, 2 * part + 3)
            nc.gpsimd.memset(h[:, 0, 0:1], 0.0).then_inc(s_spread, 1)

        @block.scalar
        def _(act):
            for q in range(QUADS):
                act.dma_start(wx_sb[quad(q)].rearrange("r k g c -> r k (g c)"),
                              Wx[hid(q), :].rearrange("(k r) n -> r k n", k=BLOCKS)).then_inc(s_wx, 16)
            act.wait_ge(s_split, 1)
            for part in range(3):
                act.dma_start(bias_f32[B * part:B * part + QUADS],
                              bias.rearrange("(g q c) -> q g c", g=GATES, q=QUADS)).then_inc(s_bias, 16)

            def step(t0, s):
                t, p = t0 + s, s % 2
                act.wait_ge(s_if, t + 1)
                nc.scalar.activation(sig_if[:, :, :], gates[0][p][:, 0:2 * HS].rearrange("p (g c) -> p g c", g=2),
                                     ACT.Sigmoid).then_inc(s_sig_if, 1)
                act.wait_ge(s_g, t + 1)
                nc.scalar.activation(tanh_g[:, :], gates[1][p][:, 0:HS], ACT.Tanh).then_inc(s_tanh_g, 1)
                act.wait_ge(s_o, t + 1)
                nc.scalar.activation(sig_o[:, :], gates[2][p][:, 0:HS], ACT.Sigmoid).then_inc(s_sig_o, 1)
                act.wait_ge(s_c, t + 1)
                nc.scalar.activation(tanh_c[:, :], c[:, :], ACT.Tanh).then_inc(s_tanh_c, 1)

            with act.Fori(0, TURNS) as turn:
                t0 = turn * ROUND
                for s in range(ROUND):
                    step(t0, s)

        @block.tensor
        def _(pe):
            def product(s, stationary, weights, first, last_sem):
                for gi, (g0, n) in enumerate(GROUPS):
                    for k in range(BLOCKS):
                        for q in range(QUADS):
                            done = nc.tensor.matmul(gates[gi][s % 2][quad(q), 0:n * HS],
                                                    stationary[:, 32 * k:32 * k + 32],
                                                    weights[:, k, g0:g0 + n, hid(q)],
                                                    start=False, stop=last_sem is not None and k == BLOCKS - 1,
                                                    skip_group_check=True)
                    if last_sem is not None:
                        done.then_inc(last_sem[gi], 1)

            def step(t0, s):
                t = t0 + s
                for gi, (g0, n) in enumerate(GROUPS):
                    nc.tensor.matmul(gates[gi][s % 2][:, 0:n * HS], spread[0:96, :],
                                     bias_parts[0:96, g0:g0 + n, :], start=True, stop=False, skip_group_check=True)
                pe.wait_ge(s_xT, t + 1)
                product(s, xT[:, s % 2, :], wx_sb, True, None)
                pe.wait_ge(s_hT, t + 1)
                product(s, hT, wh_sb, False, (s_if, s_g, s_o))

            pe.wait_ge(s_spread, 1)
            pe.wait_ge(s_parts, 3)
            pe.wait_ge(s_wx, DMA)
            pe.wait_ge(s_wh, DMA)
            with pe.Fori(0, TURNS) as turn:
                t0 = turn * ROUND
                for s in range(ROUND):
                    step(t0, s)

        @block.vector
        def _(dve):
            def transpose_x(t0, s):
                if s % CHUNK == 0:
                    slot = (s % ROUND) // CHUNK
                    dve.wait_ge(s_x[slot], (t0 + s - CHUNK * slot) * (DMA // ROUND) + DMA)
                s %= ROUND
                nc.vector.transpose(xT[:, s % 2, :], x_sb[:, s // CHUNK, s % CHUNK, :]).then_inc(s_xT, 1)

            def residual(t0, s):
                s_in = s % ROUND
                slot = s_in // CHUNK
                nc.vector.tensor_tensor(y_sb[:, slot, s_in % CHUNK, :], x_sb[:, slot, s_in % CHUNK, :],
                                        h[:, s_in % 2, :], ALU.add).then_inc(s_y, 1)

            def step(t0, s, first=False, last=False):
                t = t0 + s
                if not (last and s == ROUND - 1):
                    transpose_x(t0, s + 1)
                dve.wait_ge(s_sig_if, t + 1)
                nc.vector.tensor_tensor(fc[:, :], sig_if[:, 1, :], c[:, :], ALU.mult).then_inc(s_fc, 1)
                dve.wait_ge(s_tanh_g, t + 1)
                nc.vector.tensor_tensor(ig[:, :], sig_if[:, 0, :], tanh_g[:, :], ALU.mult).then_inc(s_ig, 1)
                dve.wait_ge(s_ig, t + 1)
                nc.vector.tensor_tensor(c[:, :], fc[:, :], ig[:, :], ALU.add).then_inc(s_c, 1)
                if not (first and s == 0):
                    prev = (s - 1) % ROUND
                    if prev % CHUNK == 0 and not first:
                        dve.wait_ge(s_stored[prev // CHUNK], t0 * (DMA // ROUND))
                    residual(t0, s - 1)
                dve.wait_ge(s_sig_o, t + 1)
                dve.wait_ge(s_tanh_c, t + 1)
                nc.vector.tensor_tensor(h[:, s % 2, :], sig_o[:, :], tanh_c[:, :], ALU.mult).then_inc(s_h, 1)
                dve.wait_ge(s_h, t + 1)
                nc.vector.transpose(hT[:, :], h[:, s % 2, :]).then_inc(s_hT, 1)

            nc.vector.memset(bias_f32[:, :, :], 0.0).then_inc(s_split, 1)
            nc.vector.memset(c[:, :], 0.0)
            dve.wait_ge(s_bias, 3 * 16)
            nc.vector.tensor_copy(bias_hi[:, :, :], bias_f32[:, :, :]).then_inc(s_split, 1)
            dve.wait_ge(s_split, 2)
            nc.vector.tensor_tensor(bias_rest[:, :, :], bias_f32[:, :, :], bias_hi[:, :, :], ALU.subtract).then_inc(s_split, 1)
            dve.wait_ge(s_split, 3)
            nc.vector.tensor_copy(bias_mid[:, :, :], bias_rest[:, :, :]).then_inc(s_split, 1)
            dve.wait_ge(s_split, 4)
            nc.vector.tensor_tensor(bias_lo[:, :, :], bias_rest[:, :, :], bias_mid[:, :, :], ALU.subtract).then_inc(s_split, 1)
            dve.wait_ge(s_split, 5)
            for part, tile in enumerate((bias_hi, bias_mid, bias_lo)):
                nc.vector.tensor_copy(bias_parts[quad(part)], tile[quad(part)]).then_inc(s_parts, 1)
            transpose_x(0, 0)
            dve.wait_ge(s_cond, DMA)
            nc.vector.transpose(hT[:, :], cond_sb[:, :]).then_inc(s_hT, 1)
            for s in range(ROUND):
                step(0, s, first=True)
            with dve.Fori(1, TURNS - 1) as turn:
                t0 = turn * ROUND
                for s in range(ROUND):
                    step(t0, s)
            for s in range(ROUND):
                step(T - ROUND, s, last=True)
            residual(T - ROUND, ROUND - 1)


_INS = ["x", "cond_1024", "L0_cond_Wx", "L0_cond_Wh", "L0_cond_b"]


def kernel(**inputs):
    import numpy as _np
    import concourse.bacc as _bacc
    from concourse import mybir as _mybir
    from concourse.bass_utils import run_bass_kernel_spmd as _run

    nc = _bacc.Bacc("TRN2", target_bir_lowering=False, num_devices=1)
    arrays, args = {}, []
    for name in _INS:
        a = _np.ascontiguousarray(inputs[name])
        arrays[f"in_{name}"] = a
        args.append(nc.dram_tensor(f"in_{name}", a.shape, _mybir.dt.from_np(a.dtype), kind="ExternalInput").ap())
    shape = arrays["in_x"].shape
    args.append(nc.dram_tensor("out_y", shape, _mybir.dt.from_np(arrays["in_x"].dtype), kind="ExternalOutput").ap())
    lstm_residual(nc, *args)
    r = _run(nc, [arrays], core_ids=[0])
    return r.results[0]["out_y"]
```

```python
from contextlib import ExitStack

import concourse.bass as bass
from concourse import mybir

F32 = mybir.dt.float32
F16 = mybir.dt.float16
BF16 = mybir.dt.bfloat16
I32 = mybir.dt.int32
ACT = mybir.ActivationFunctionType
ALU = mybir.AluOpType
AX_X = mybir.AxisListType.X

P = 128
B, T, D = 32, 256, 256
H = 256
GATES = 4
QUADS = P // B
HS = H // QUADS
BLOCKS = H // P
HB = BLOCKS * B
CHUNK = 8
SLOTS = 2
ROUND = CHUNK * SLOTS
ROUNDS = T // ROUND
ACT_STEPS = 4 * ROUND
DMA = 16 * QUADS

GATE_I, GATE_F, GATE_O, GATE_G = range(GATES)
ORDER = (GATE_G, GATE_I, GATE_F, GATE_O)
H_SCALE = 2.0 ** 14
W_TOP = 2.0 ** 14
W_LEAST = 2.0 ** -20
EXPONENT = 0x7F800000
PARTS = 3


def lstm_residual(nc, x, cond, Wx, Wh, bias, out):
    ctx = ExitStack()
    with ctx:
        def sb(name, shape, dt=F32):
            return ctx.enter_context(nc.sbuf_tensor(name, shape, dt))

        def sem(name):
            return ctx.enter_context(nc.semaphore(name))

        wx_raw = sb("wx_raw", [P, BLOCKS, GATES * H])
        wh_raw = sb("wh_raw", [P, BLOCKS, GATES * H])
        wx_sb = sb("wx_sb", [P, BLOCKS, BLOCKS, GATES, P])
        wh_hi = sb("wh_hi", [P, BLOCKS, BLOCKS, GATES, P], F16)
        wh_lo = sb("wh_lo", [P, BLOCKS, BLOCKS, GATES, P], F16)
        w_max = sb("w_max", [P, 1])
        w_all_max = sb("w_all_max", [P, 1])
        w_clamped = sb("w_clamped", [P, 1])
        w_pow2 = sb("w_pow2", [P, 1])
        w_inv = sb("w_inv", [P, 1])
        w_scale = sb("w_scale", [P, 1])
        full_scale = sb("full_scale", [P, 1])
        un_scale = sb("un_scale", [P, 1])
        bias_raw = sb("bias_raw", [P, GATES * H])
        bias_scaled = sb("bias_scaled", [P, BLOCKS, GATES, P])
        bias_rest = sb("bias_rest", [P, BLOCKS, GATES, P])
        bias_hi = sb("bias_hi", [P, BLOCKS, GATES, P], BF16)
        bias_mid = sb("bias_mid", [P, BLOCKS, GATES, P], BF16)
        bias_parts = sb("bias_parts", [P, BLOCKS, GATES, P], BF16)
        ones = sb("ones", [P, CHUNK * B], BF16)
        cond_sb = sb("cond_sb", [P, HS])
        cond_T = sb("cond_T", [P, HB])
        cond_scaled = sb("cond_scaled", [P, HB])
        cond_rest = sb("cond_rest", [P, HB])
        cond_parts = sb("cond_parts", [P, PARTS, HB], BF16)
        x_sb = sb("x_sb", [P, SLOTS, CHUNK, HS])
        xT = sb("xT", [P, SLOTS, CHUNK, BLOCKS, B])
        yT = sb("yT", [P, SLOTS, CHUNK, HB])
        y_sb = sb("y_sb", [P, SLOTS, CHUNK, HS])
        h_hi = sb("h_hi", [P, HB], F16)
        h_lo = sb("h_lo", [P, HB], F16)
        h_f32 = sb("h_f32", [P, HB])
        c = sb("c", [P, HB])
        tanh_g = sb("tanh_g", [P, HB])
        sig_i = sb("sig_i", [P, HB])
        sig_f = sb("sig_f", [P, HB])
        sig_o = sb("sig_o", [P, HB])
        tanh_c = sb("tanh_c", [P, HB])
        ig = sb("ig", [P, HB])
        fc = sb("fc", [P, HB])

        gates = [[ctx.enter_context(nc.psum_tensor(f"gate{g}_{s}", [P, BLOCKS, CHUNK, B], F32))
                  for g in range(GATES)] for s in range(SLOTS)]

        s_wx = sem("wx_loaded")
        s_wh = sem("wh_loaded")
        s_bias = sem("bias_loaded")
        s_cond = sem("cond_loaded")
        s_x = [sem(f"x_loaded{s}") for s in range(SLOTS)]
        s_stored = [sem(f"y_stored{s}") for s in range(SLOTS)]
        s_wmax = sem("w_max_ready")
        s_all_max = sem("w_all_max_ready")
        s_scale = sem("scale_steps")
        s_wx_scaled = sem("wx_scaled")
        s_whi = sem("wh_hi_ready")
        s_wlo = sem("wh_lo_ready")
        s_zero = sem("bias_rows_zeroed")
        s_bstep = sem("bias_split_steps")
        s_bparts = sem("bias_parts_ready")
        s_cstep = sem("cond_split_steps")
        s_cparts = sem("cond_parts_ready")
        s_czero = sem("c_zeroed")
        s_xT = sem("xT_ready")
        s_gate = {g: sem(f"{n}_in_psum") for g, n in zip(ORDER, "gifo")}
        s_tanh_g = sem("tanh_g_ready")
        s_sig_i = sem("sig_i_ready")
        s_sig_f = sem("sig_f_ready")
        s_sig_o = sem("sig_o_ready")
        s_tanh_c = sem("tanh_c_ready")
        s_ig = sem("ig_ready")
        s_fc = sem("fc_ready")
        s_c = sem("c_ready")
        s_hi = sem("h_hi_ready")
        s_h = sem("h_f32_ready")
        s_lo = sem("h_lo_ready")
        s_yT = sem("yT_ready")
        s_y = sem("y_ready")

        block = ctx.enter_context(nc.Block())

        def quad(q):
            return slice(B * q, B * q + B)

        def hid(q):
            return slice(HS * q, HS * q + HS)

        def by_block(raw, m):
            return raw.rearrange("p (gq m r) -> p m gq r", m=BLOCKS, r=B)[:, m]

        def packed(tile):
            return tile.rearrange("p g (q r) -> p (g q) r", r=B)

        @block.sync
        def _(sp):
            def load_x(t0, slot):
                for q in range(QUADS):
                    sp.dma_start(x_sb[quad(q), slot], x[:, bass.ds(t0, CHUNK), hid(q)]).then_inc(s_x[slot], 16)

            def store_y(t0, slot):
                for q in range(QUADS):
                    sp.dma_start(out[:, bass.ds(t0, CHUNK), hid(q)], y_sb[quad(q), slot]).then_inc(s_stored[slot], 16)

            for q in range(0, QUADS, 2):
                sp.dma_start(wh_raw[quad(q)], Wh[hid(q), :].rearrange("(k r) n -> r k n", k=BLOCKS)).then_inc(s_wh, 16)
            load_x(0, 0)
            for q in range(QUADS):
                sp.dma_start(cond_sb[quad(q), :], cond[:, hid(q)]).then_inc(s_cond, 16)
            for q in range(0, QUADS, 2):
                sp.dma_start(wx_raw[quad(q)], Wx[hid(q), :].rearrange("(k r) n -> r k n", k=BLOCKS)).then_inc(s_wx, 16)
            load_x(CHUNK, 1)

            with sp.Fori(0, ROUNDS - 1) as turn:
                t0 = turn * ROUND
                for slot in range(SLOTS):
                    sp.wait_ge(s_xT, turn * SLOTS + slot + 1)
                    load_x(t0 + ROUND + CHUNK * slot, slot)
                    sp.wait_ge(s_y, turn * SLOTS + slot + 1)
                    store_y(t0 + CHUNK * slot, slot)
            for slot in range(SLOTS):
                sp.wait_ge(s_y, (ROUNDS - 1) * SLOTS + slot + 1)
                store_y(T - ROUND + CHUNK * slot, slot)
            for slot in range(SLOTS):
                sp.wait_ge(s_stored[slot], DMA * ROUNDS)

        @block.gpsimd
        def _(pool):
            nc.gpsimd.memset(bias_raw[:, :], 0.0).then_inc(s_zero, 1)
            pool.wait_ge(s_wmax, 1)
            nc.gpsimd.partition_all_reduce(w_all_max[:, :], w_max[:, :], P, bass.bass_isa.ReduceOp.max).then_inc(s_all_max, 1)
            nc.gpsimd.memset(ones[:, :], 1.0).then_inc(s_bstep, 1)
            pool.wait_ge(s_bias, 16 * PARTS)
            pool.wait_ge(s_scale, 6)
            for m in range(BLOCKS):
                nc.gpsimd.tensor_scalar(packed(bias_scaled[:, m]), by_block(bias_raw[:, :], m), full_scale[:, 0:1],
                                        None, ALU.mult).then_inc(s_bstep, 1)
            pool.wait_ge(s_bstep, 3)
            nc.gpsimd.tensor_copy(bias_hi[:], bias_scaled[:]).then_inc(s_bstep, 1)
            pool.wait_ge(s_bstep, 4)
            nc.gpsimd.tensor_tensor(bias_rest[:], bias_scaled[:], bias_hi[:], ALU.subtract).then_inc(s_bstep, 1)
            pool.wait_ge(s_bstep, 5)
            nc.gpsimd.tensor_copy(bias_mid[:], bias_rest[:]).then_inc(s_bstep, 1)
            pool.wait_ge(s_bstep, 6)
            nc.gpsimd.tensor_tensor(bias_parts[:], bias_rest[:], bias_mid[:], ALU.subtract).then_inc(s_bstep, 1)
            pool.wait_ge(s_bstep, 7)
            nc.gpsimd.tensor_copy(bias_parts[quad(0)], bias_hi[quad(0)]).then_inc(s_bparts, 1)
            nc.gpsimd.tensor_copy(bias_parts[quad(1)], bias_mid[quad(1)]).then_inc(s_bparts, 1)

        @block.scalar
        def _(act):
            for q in range(1, QUADS, 2):
                act.dma_start(wh_raw[quad(q)], Wh[hid(q), :].rearrange("(k r) n -> r k n", k=BLOCKS)).then_inc(s_wh, 16)
            for q in range(1, QUADS, 2):
                act.dma_start(wx_raw[quad(q)], Wx[hid(q), :].rearrange("(k r) n -> r k n", k=BLOCKS)).then_inc(s_wx, 16)
            act.wait_ge(s_zero, 1)
            for part in range(PARTS):
                act.dma_start(bias_raw[B * part:B * part + 1, :], bias.rearrange("(a n) -> a n", a=1)).then_inc(s_bias, 16)

            act.wait_ge(s_scale, 6)
            act.wait_ge(s_wx, DMA)
            for k in range(BLOCKS):
                nc.scalar.activation(packed(wx_sb[:, k, 0]), by_block(wx_raw[:, k], 0), ACT.Copy,
                                     scale=full_scale[:, 0:1]).then_inc(s_wx_scaled, 1)
            for k in range(BLOCKS):
                for m in range(BLOCKS):
                    nc.scalar.activation(packed(wh_hi[:, k, m]), by_block(wh_raw[:, k], m), ACT.Copy,
                                         scale=w_scale[:, 0:1]).then_inc(s_whi, 1)
            unscale = act.alloc_register("unscale")
            act.reg_load(unscale, un_scale[0:1, 0:1].bitcast(I32))

            def step(t0, s):
                t, slot, col = t0 + s, s % ROUND // CHUNK, s % CHUNK
                for g, func, dst, done in ((GATE_G, ACT.Tanh, tanh_g, s_tanh_g), (GATE_I, ACT.Sigmoid, sig_i, s_sig_i),
                                           (GATE_F, ACT.Sigmoid, sig_f, s_sig_f), (GATE_O, ACT.Sigmoid, sig_o, s_sig_o)):
                    act.wait_ge(s_gate[g], t + 1)
                    nc.scalar.activation(dst[:, :].rearrange("p (m b) -> p m b", m=BLOCKS), gates[slot][g][:, :, col, :],
                                         func, scale=unscale).then_inc(done, 1)
                act.wait_ge(s_c, t + 1)
                nc.scalar.activation(tanh_c[:, :], c[:, :], ACT.Tanh).then_inc(s_tanh_c, 1)

            with act.Fori(0, T // ACT_STEPS) as turn:
                t0 = turn * ACT_STEPS
                for s in range(ACT_STEPS):
                    step(t0, s)

        @block.tensor
        def _(pe):
            def project(slot, g, m):
                dst = gates[slot][g][:, m, :, :]
                for k in range(BLOCKS):
                    nc.tensor.matmul(dst, wx_sb[:, k, m, g], xT[:, slot, :, k, :],
                                     start=(m == 0 and k == 0), stop=False, skip_group_check=True)

            def add_bias(slot, g, m):
                return nc.tensor.matmul(gates[slot][g][:, m, :, :], bias_parts[:, m, g],
                                 ones[:, :].rearrange("p (s b) -> p s b", b=B),
                                 start=False, stop=False, skip_group_check=True)

            def accumulate(slot, col, g, weights, state, done=None):
                for m in range(BLOCKS):
                    for k in range(BLOCKS):
                        last = nc.tensor.matmul(gates[slot][g][:, m, col, :], weights[:, k, m, g], state[:, quad(k)],
                                                start=False, stop=done is not None, skip_group_check=True)
                if done is not None:
                    last.then_inc(done, 1)

            def step(turn, s, last=False):
                t, slot, col = turn * ROUND + s, s // CHUNK, s % CHUNK
                pe.wait_ge(s_hi, t)
                for g in ORDER[:3]:
                    accumulate(slot, col, g, wh_hi, h_hi)
                    accumulate(slot, col, g, wh_lo, h_hi)
                pe.wait_ge(s_lo, t)
                for g in ORDER[:3]:
                    accumulate(slot, col, g, wh_hi, h_lo, s_gate[g])
                g = ORDER[3]
                accumulate(slot, col, g, wh_hi, h_hi)
                accumulate(slot, col, g, wh_lo, h_hi)
                accumulate(slot, col, g, wh_hi, h_lo, s_gate[g])
                if not (last and slot == SLOTS - 1):
                    project_ahead(turn, s)

            def project_ahead(turn, s):
                slot, col = s // CHUNK, s % CHUNK
                if col == 0:
                    pe.wait_ge(s_xT, turn * SLOTS + slot + 2)
                project(1 - slot, ORDER[col // BLOCKS], col % BLOCKS)
                add_bias(1 - slot, ORDER[col // BLOCKS], col % BLOCKS)

            pe.wait_ge(s_wx_scaled, 2 * BLOCKS)
            pe.wait_ge(s_xT, 1)
            for g in ORDER:
                for m in range(BLOCKS):
                    project(0, g, m)
            pe.wait_ge(s_cparts, PARTS)
            pe.wait_ge(s_whi, BLOCKS * BLOCKS)
            pe.wait_ge(s_wlo, BLOCKS * BLOCKS)
            for g in ORDER:
                for part in range(PARTS):
                    accumulate(0, 0, g, wh_hi, cond_parts[:, part])
                    accumulate(0, 0, g, wh_lo, cond_parts[:, part])
            pe.wait_ge(s_bparts, 2)
            for g in ORDER:
                for m in range(BLOCKS):
                    last = add_bias(0, g, m)
                last.then_inc(s_gate[g], 1)
            project_ahead(0, 0)
            for s in range(1, ROUND):
                step(0, s)
            with pe.Fori(1, ROUNDS - 1) as turn:
                for s in range(ROUND):
                    step(turn, s)
            for s in range(ROUND):
                step(ROUNDS - 1, s, last=True)

        @block.vector
        def _(dve):
            def transpose_x(slot, loads):
                dve.wait_ge(s_x[slot], DMA * loads)
                nc.vector.transpose(xT[:, slot].rearrange("p t k b -> p (t k b)"),
                                    x_sb[:, slot].rearrange("p t c -> p (t c)")).then_inc(s_xT, 1)

            def residual(t, s):
                slot, col = s // CHUNK, s % CHUNK
                dve.wait_ge(s_h, t + 1)
                nc.vector.scalar_tensor_tensor(yT[:, slot, col], h_f32[:, :], 1.0 / H_SCALE,
                                               xT[:, slot, col].rearrange("p k b -> p (k b)"),
                                               ALU.mult, ALU.add).then_inc(s_yT, 1)

            def transpose_y(t_next, slot):
                dve.wait_ge(s_yT, t_next)
                nc.vector.transpose(y_sb[:, slot].rearrange("p t c -> p (t c)"),
                                    yT[:, slot].rearrange("p t c -> p (t c)")).then_inc(s_y, 1)

            def step(turn, s, first=False, last=False):
                t, slot, col = turn * ROUND + s, s // CHUNK, s % CHUNK
                if not (first and s == 0):
                    residual(t - 1, (s - 1) % ROUND)
                if col == 0 and not (last and slot == SLOTS - 1):
                    if not (first and s == 0):
                        dve.wait_ge(s_yT, t)
                    transpose_x(1 - slot, turn + 1 + slot)
                if col == 1 and not (first and slot == 0):
                    wait_stored(turn - 1 if slot == 0 else turn, 1 - slot)
                    transpose_y(t - 1, 1 - slot)
                dve.wait_ge(s_sig_i, t + 1)
                nc.vector.tensor_tensor(ig[:, :], tanh_g[:, :], sig_i[:, :], ALU.mult).then_inc(s_ig, 1)
                dve.wait_ge(s_sig_f, t + 1)
                nc.vector.tensor_tensor(fc[:, :], sig_f[:, :], c[:, :], ALU.mult).then_inc(s_fc, 1)
                dve.wait_ge(s_fc, t + 1)
                nc.vector.tensor_tensor(c[:, :], fc[:, :], ig[:, :], ALU.add).then_inc(s_c, 1)
                dve.wait_ge(s_tanh_c, t + 1)
                nc.vector.scalar_tensor_tensor(h_hi[:, :], sig_o[:, :], H_SCALE, tanh_c[:, :],
                                               ALU.mult, ALU.mult).then_inc(s_hi, 1)
                nc.vector.scalar_tensor_tensor(h_f32[:, :], sig_o[:, :], H_SCALE, tanh_c[:, :],
                                               ALU.mult, ALU.mult).then_inc(s_h, 1)
                dve.wait_ge(s_h, t + 1)
                nc.vector.tensor_tensor(h_lo[:, :], h_f32[:, :], h_hi[:, :], ALU.subtract).then_inc(s_lo, 1)

            def wait_stored(turn, slot):
                if isinstance(turn, int) and turn == 0:
                    return
                dve.wait_ge(s_stored[slot], turn * DMA)

            nc.vector.memset(c[:, :], 0.0).then_inc(s_czero, 1)
            dve.wait_ge(s_wh, DMA)
            nc.vector.tensor_reduce(w_max[:, :], wh_raw[:, :, :].rearrange("p k n -> p (k n)"), AX_X, ALU.max,
                                    apply_absolute_value=True).then_inc(s_wmax, 1)
            dve.wait_ge(s_cond, DMA)
            nc.vector.transpose(cond_T[:, :], cond_sb[:, :]).then_inc(s_cstep, 1)
            transpose_x(0, 1)
            dve.wait_ge(s_all_max, 1)
            nc.vector.tensor_scalar(w_clamped[:, :], w_all_max[:, :], W_LEAST, None, ALU.max).then_inc(s_scale, 1)
            dve.wait_ge(s_scale, 1)
            nc.vector.tensor_scalar(w_pow2[:, :].bitcast(I32), w_clamped[:, :].bitcast(I32), EXPONENT, None,
                                    ALU.bitwise_and).then_inc(s_scale, 1)
            dve.wait_ge(s_scale, 2)
            nc.vector.reciprocal(w_inv[:, :], w_pow2[:, :]).then_inc(s_scale, 1)
            nc.vector.tensor_scalar(un_scale[:, :], w_pow2[:, :], 1.0 / (W_TOP * H_SCALE), None, ALU.mult).then_inc(s_scale, 1)
            dve.wait_ge(s_scale, 4)
            nc.vector.tensor_scalar(w_scale[:, :], w_inv[:, :], W_TOP, None, ALU.mult).then_inc(s_scale, 1)
            nc.vector.tensor_scalar(full_scale[:, :], w_inv[:, :], W_TOP * H_SCALE, None, ALU.mult).then_inc(s_scale, 1)
            dve.wait_ge(s_scale, 6)
            dve.wait_ge(s_wx, DMA)
            for k in range(BLOCKS):
                nc.vector.tensor_scalar(packed(wx_sb[:, k, 1]), by_block(wx_raw[:, k], 1), full_scale[:, 0:1],
                                        None, ALU.mult).then_inc(s_wx_scaled, 1)

            dve.wait_ge(s_cstep, 1)
            nc.vector.tensor_scalar(cond_scaled[:, :], cond_T[:, :], H_SCALE, None, ALU.mult).then_inc(s_cstep, 1)
            dve.wait_ge(s_cstep, 2)
            nc.vector.tensor_copy(cond_parts[:, 0], cond_scaled[:, :]).then_inc(s_cparts, 1)
            dve.wait_ge(s_cparts, 1)
            nc.vector.tensor_tensor(cond_rest[:, :], cond_scaled[:, :], cond_parts[:, 0], ALU.subtract).then_inc(s_cstep, 1)
            dve.wait_ge(s_cstep, 3)
            nc.vector.tensor_copy(cond_parts[:, 1], cond_rest[:, :]).then_inc(s_cparts, 1)
            dve.wait_ge(s_cparts, 2)
            nc.vector.tensor_tensor(cond_parts[:, 2], cond_rest[:, :], cond_parts[:, 1], ALU.subtract).then_inc(s_cparts, 1)

            for k in range(BLOCKS):
                for m in range(BLOCKS):
                    dve.wait_ge(s_whi, k * BLOCKS + m + 1)
                    nc.vector.scalar_tensor_tensor(packed(wh_lo[:, k, m]), by_block(wh_raw[:, k], m), w_scale[:, 0:1],
                                                   packed(wh_hi[:, k, m]), ALU.mult, ALU.subtract).then_inc(s_wlo, 1)

            dve.wait_ge(s_czero, 1)
            for s in range(ROUND):
                step(0, s, first=True)
            with dve.Fori(1, ROUNDS - 1) as turn:
                for s in range(ROUND):
                    step(turn, s)
            for s in range(ROUND):
                step(ROUNDS - 1, s, last=True)
            residual(T - 1, ROUND - 1)
            wait_stored(ROUNDS - 1, SLOTS - 1)
            transpose_y(T, SLOTS - 1)


_INS = ["x", "cond_1024", "L0_cond_Wx", "L0_cond_Wh", "L0_cond_b"]


def kernel(**inputs):
    import numpy as _np
    import concourse.bacc as _bacc
    from concourse import mybir as _mybir
    from concourse.bass_utils import run_bass_kernel_spmd as _run

    nc = _bacc.Bacc("TRN2", target_bir_lowering=False, num_devices=1)
    arrays, args = {}, []
    for name in _INS:
        a = _np.ascontiguousarray(inputs[name])
        arrays[f"in_{name}"] = a
        args.append(nc.dram_tensor(f"in_{name}", a.shape, _mybir.dt.from_np(a.dtype), kind="ExternalInput").ap())
    shape = arrays["in_x"].shape
    args.append(nc.dram_tensor("out_y", shape, _mybir.dt.from_np(arrays["in_x"].dtype), kind="ExternalOutput").ap())
    lstm_residual(nc, *args)
    r = _run(nc, [arrays], core_ids=[0])
    return r.results[0]["out_y"]
```

```python
from contextlib import ExitStack

import concourse.bass as bass
from concourse import mybir

F32 = mybir.dt.float32
F16 = mybir.dt.float16
BF16 = mybir.dt.bfloat16
F32R = mybir.dt.float32r
I32 = mybir.dt.int32
ACT = mybir.ActivationFunctionType
ALU = mybir.AluOpType
AX_X = mybir.AxisListType.X

P = 128
B, T = 32, 256
H = 256
GATES = 4
QUADS = P // B
HS = H // QUADS
BLOCKS = H // P
HB = BLOCKS * B
CHUNK = 8
SLOTS = 2
ROUND = CHUNK * SLOTS
ROUNDS = T // ROUND
DVE_TURN = 6
ACT_STEPS = 4 * ROUND
DMA = 16 * QUADS

GATE_I, GATE_F, GATE_O, GATE_G = range(GATES)
REGIONS = {(GATE_I, 0): 0, (GATE_F, 0): 1, (GATE_I, 1): 2, (GATE_F, 1): 3,
           (GATE_G, 0): 4, (GATE_G, 1): 5, (GATE_O, 0): 6, (GATE_O, 1): 7}
HALVES = (range(0, CHUNK // 2), range(CHUNK // 2, CHUNK))
LAST_PIECES = (range(0, CHUNK - 4), range(CHUNK - 4, CHUNK - 2), range(CHUNK - 2, CHUNK))
H_SCALE = 2.0 ** 14
W_TOP = 2.0 ** 14
W_LEAST = 2.0 ** -20
EXPONENT = 0x7F800000
WARM_UP = 27
PARTS = 3


def lstm_residual(nc, x, cond, Wx, Wh, bias, out):
    ctx = ExitStack()
    with ctx:
        def sb(name, shape, dt=F32):
            return ctx.enter_context(nc.sbuf_tensor(name, shape, dt))

        def sem(name):
            return ctx.enter_context(nc.semaphore(name))

        wx_raw = sb("wx_raw", [P, BLOCKS, GATES * H])
        wh_raw = sb("wh_raw", [P, BLOCKS, GATES * H])
        wx_hi = sb("wx_hi", [P, BLOCKS, BLOCKS, GATES, P], F32R)
        wx_lo = sb("wx_lo", [P, BLOCKS, BLOCKS, GATES, P], F32R)
        wh_hi = sb("wh_hi", [P, BLOCKS, BLOCKS, GATES, P], F16)
        wh_lo = sb("wh_lo", [P, BLOCKS, BLOCKS, GATES, P], F16)
        w_max_of = sb("w_max_of", [P, BLOCKS])
        w_max = sb("w_max", [P, 1])
        w_all_max = sb("w_all_max", [P, 1])
        w_clamped = sb("w_clamped", [P, 1])
        w_pow2 = sb("w_pow2", [P, 1])
        w_inv = sb("w_inv", [P, 1])
        w_scale = sb("w_scale", [P, 1])
        full_scale = sb("full_scale", [P, 1])
        un_scale = sb("un_scale", [P, 1])
        bias_raw = sb("bias_raw", [B, B])
        bias_scaled = sb("bias_scaled", [B, B])
        bias_rest = sb("bias_rest", [B, B])
        bias_cut = sb("bias_cut", [B, PARTS, B], BF16)
        bias_parts = sb("bias_parts", [P, BLOCKS, GATES, P], BF16)
        ones = sb("ones", [P, CHUNK * B], BF16)
        cond_sb = sb("cond_sb", [P, HS])
        cond_T = sb("cond_T", [P, HB])
        cond_scaled = sb("cond_scaled", [P, HB])
        cond_rest = sb("cond_rest", [P, HB])
        cond_parts = sb("cond_parts", [P, PARTS, HB], BF16)
        x_sb = sb("x_sb", [P, SLOTS, CHUNK, HS])
        xT = sb("xT", [P, SLOTS, CHUNK, BLOCKS, B])
        xT_hi = sb("xT_hi", [P, BLOCKS, CHUNK, B], F32R)
        xT_lo = sb("xT_lo", [P, BLOCKS, CHUNK, B], F32R)
        yT = sb("yT", [P, SLOTS, CHUNK, HB])
        y_sb = sb("y_sb", [P, SLOTS, CHUNK, HS])
        h_hi = sb("h_hi", [P, HB], F16)
        h_lo = sb("h_lo", [P, HB], F16)
        h_f32 = sb("h_f32", [P, HB])
        gc = sb("gc", [P, BLOCKS, 2, B])
        sig_if = sb("sig_if", [P, BLOCKS, 2, B])
        prod = sb("prod", [P, BLOCKS, 2, B])
        sig_o = sb("sig_o", [P, HB])
        tanh_c = sb("tanh_c", [P, HB])

        gates = [ctx.enter_context(nc.psum_tensor(f"gates{s}", [P, len(REGIONS), CHUNK, B], F32))
                 for s in range(SLOTS)]
        table = sb("table", [1, 1])

        s_wx = [sem(f"wx_loaded{k}") for k in range(BLOCKS)]
        s_wh = [sem(f"wh_loaded{k}") for k in range(BLOCKS)]
        s_bias = sem("bias_loaded")
        s_cond = sem("cond_loaded")
        s_x = [sem(f"x_loaded{s}") for s in range(SLOTS)]
        s_stored = [sem(f"y_stored{s}") for s in range(SLOTS)]
        s_wmax = sem("w_max_ready")
        s_all_max = sem("w_all_max_ready")
        s_scale = sem("scale_steps")
        s_wxhi = sem("wx_hi_ready")
        s_wxlo = [sem(f"wx_lo{k}_ready") for k in range(BLOCKS)]
        s_whi = sem("wh_hi_ready")
        s_wlo = sem("wh_lo_ready")
        s_ones = sem("ones_ready")
        s_zeroed = sem("bias_parts_zeroed")
        s_bstep = sem("bias_split_steps")
        s_bcut = sem("bias_cut")
        s_bparts = sem("bias_parts_in_rows")
        s_cstep = sem("cond_split_steps")
        s_cparts = sem("cond_parts_ready")
        s_czero = sem("c_zeroed")
        s_table = sem("function_table_in")
        s_xT = sem("xT_ready")
        s_xhi = sem("xT_hi_ready")
        s_xlo = sem("xT_lo_ready")
        s_pg = sem("g_in_psum")
        s_pif = [sem(f"if{m}_in_psum") for m in range(BLOCKS)]
        s_po = sem("o_in_psum")
        s_sig_if = [sem(f"sig_if{m}_ready") for m in range(BLOCKS)]
        s_sig_o = sem("sig_o_ready")
        s_tanh_g = sem("tanh_g_ready")
        s_tanh_c = [sem(f"tanh_c{m}_ready") for m in range(BLOCKS)]
        s_prod = [sem(f"prod{m}_ready") for m in range(BLOCKS)]
        s_c = [sem(f"c{m}_ready") for m in range(BLOCKS)]
        s_hi = [sem(f"h_hi{m}_ready") for m in range(BLOCKS)]
        s_h = [sem(f"h_f32_{m}_ready") for m in range(BLOCKS)]
        s_lo = [sem(f"h_lo{m}_ready") for m in range(BLOCKS)]
        s_yT = sem("yT_ready")
        s_y = sem("y_ready")

        block = ctx.enter_context(nc.Block())

        def quad(q):
            return slice(B * q, B * q + B)

        def hid(q):
            return slice(HS * q, HS * q + HS)

        def by_block(raw, m):
            return raw.rearrange("p (gq m r) -> p m gq r", m=BLOCKS, r=B)[:, m]

        def packed(tile):
            return tile.rearrange("p g (q r) -> p (g q) r", r=B)

        def load_x(t0, slot, q, engine=nc.sync):
            engine.dma_start(x_sb[quad(q), slot], x[:, bass.ds(t0, CHUNK), hid(q)]).then_inc(s_x[slot], 16)

        def load_block(engine, raw, weights, k, loaded):
            engine.dma_start(raw[:, k], weights.rearrange("(q k r) n -> k q r n", k=BLOCKS, r=B)[k]).then_inc(loaded, 16)

        def rest_wx(engine, k, m):
            engine.tensor_tensor(packed(wx_lo[:, k, m]), by_block(wx_raw[:, k], m),
                                 packed(wx_hi[:, k, m]).bitcast(F32), ALU.subtract).then_inc(s_wxlo[k], 1)

        def store_step(engine, col):
            engine.dma_start(out[:, T - CHUNK + col, :].rearrange("b (q c) -> q b c", q=QUADS),
                             y_sb[:, SLOTS - 1, col]).then_inc(s_stored[SLOTS - 1], 16)

        @block.sync
        def _(sp):
            def store_y(t0, slot):
                for q in range(QUADS):
                    sp.dma_start(out[:, bass.ds(t0, CHUNK), hid(q)], y_sb[quad(q), slot]).then_inc(s_stored[slot], 16)

            load_block(sp, wh_raw, Wh, 0, s_wh[0])
            sp.dma_start(cond_sb[:, :], cond.rearrange("b (q c) -> q b c", q=QUADS)).then_inc(s_cond, 16)
            sp.dma_start(bias_raw[:, :], bias.rearrange("(gq m r) -> m gq r", m=BLOCKS, r=B)).then_inc(s_bias, 16)
            load_block(sp, wx_raw, Wx, 0, s_wx[0])
            load_x(0, 0, 0)
            for q in range(QUADS):
                load_x(CHUNK, 1, q)

            sp.wait_ge(s_zeroed, 1)
            sp.wait_ge(s_bcut, 1)
            for part in range(PARTS):
                sp.dma_start(bias_parts[B * part:B * part + 1].rearrange("p m g n -> p (m g n)"),
                             bias_cut[:, part]).then_inc(s_bparts, 16)

            for slot in range(SLOTS):
                sp.wait_ge(s_xT, (slot + 1) * BLOCKS)
                for q in range(QUADS):
                    load_x(ROUND + CHUNK * slot, slot, q)
            with sp.Fori(0, ROUNDS - 2) as turn:
                t0 = turn * ROUND
                for slot in range(SLOTS):
                    sp.wait_ge(s_xT, (turn * SLOTS + SLOTS + slot + 1) * BLOCKS)
                    for q in range(QUADS):
                        load_x(t0 + 2 * ROUND + CHUNK * slot, slot, q)
                    sp.wait_ge(s_y, (turn * SLOTS + slot + 1) * 2)
                    store_y(t0 + CHUNK * slot, slot)
            for chunk in range((ROUNDS - 2) * SLOTS, ROUNDS * SLOTS - 1):
                sp.wait_ge(s_y, (chunk + 1) * 2)
                store_y(chunk * CHUNK, chunk % SLOTS)
            for piece, cols in enumerate(LAST_PIECES):
                sp.wait_ge(s_y, (T // CHUNK - 1) * 2 + piece + 1)
                for col in cols:
                    if col < CHUNK - 1:
                        store_step(sp, col)
            sp.wait_ge(s_stored[0], DMA * ROUNDS)
            sp.wait_ge(s_stored[SLOTS - 1], DMA * (ROUNDS - 1) + 16 * CHUNK)

        @block.gpsimd
        def _(pool):
            nc.gpsimd.memset(bias_parts[:].bitcast(I32), 0).then_inc(s_zeroed, 1)
            pool.wait_ge(s_wmax, BLOCKS + 1)
            nc.gpsimd.partition_all_reduce(w_all_max[:, :], w_max[:, :], P, bass.bass_isa.ReduceOp.max).then_inc(s_all_max, 1)
            pool.wait_ge(s_bias, 16)
            pool.wait_ge(s_scale, 6)
            nc.gpsimd.tensor_scalar(bias_scaled[:, :], bias_raw[:, :], full_scale[0:B, 0:1], None, ALU.mult).then_inc(s_bstep, 1)
            pool.wait_ge(s_bstep, 1)
            nc.gpsimd.tensor_copy(bias_cut[:, 0], bias_scaled[:, :]).then_inc(s_bstep, 1)
            pool.wait_ge(s_bstep, 2)
            nc.gpsimd.tensor_tensor(bias_rest[:, :], bias_scaled[:, :], bias_cut[:, 0], ALU.subtract).then_inc(s_bstep, 1)
            pool.wait_ge(s_bstep, 3)
            nc.gpsimd.tensor_copy(bias_cut[:, 1], bias_rest[:, :]).then_inc(s_bstep, 1)
            pool.wait_ge(s_bstep, 4)
            nc.gpsimd.tensor_tensor(bias_cut[:, 2], bias_rest[:, :], bias_cut[:, 1], ALU.subtract).then_inc(s_bcut, 1)
            pool.wait_ge(s_cstep, 1)
            nc.gpsimd.tensor_scalar(cond_scaled[:, :], cond_T[:, :], H_SCALE, None, ALU.mult).then_inc(s_cstep, 1)
            pool.wait_ge(s_cstep, 2)
            nc.gpsimd.tensor_copy(cond_parts[:, 0], cond_scaled[:, :]).then_inc(s_cparts, 1)
            pool.wait_ge(s_cparts, 1)
            nc.gpsimd.tensor_tensor(cond_rest[:, :], cond_scaled[:, :], cond_parts[:, 0], ALU.subtract).then_inc(s_cstep, 1)
            pool.wait_ge(s_cstep, 3)
            nc.gpsimd.tensor_copy(cond_parts[:, 1], cond_rest[:, :]).then_inc(s_cparts, 1)
            pool.wait_ge(s_cparts, 2)
            nc.gpsimd.tensor_tensor(cond_parts[:, 2], cond_rest[:, :], cond_parts[:, 1], ALU.subtract).then_inc(s_cparts, 1)
            for m in range(BLOCKS):
                pool.wait_ge(s_wxhi, BLOCKS + m + 1)
                rest_wx(nc.gpsimd, 1, m)

        @block.scalar
        def _(act):
            load_block(act, wh_raw, Wh, 1, s_wh[1])
            for q in range(1, QUADS):
                load_x(0, 0, q, act)
            load_block(act, wx_raw, Wx, 1, s_wx[1])

            def cut_x(slot, chunk, k):
                act.wait_ge(s_xT, chunk * BLOCKS + k + 1)
                nc.scalar.activation(xT_hi[:, k], xT[:, slot, :, k, :], ACT.Copy,
                                     scale=full_scale[:, 0:1]).then_inc(s_xhi, 1)

            def cut_wh(k):
                for m in range(BLOCKS):
                    nc.scalar.activation(packed(wh_hi[:, k, m]), by_block(wh_raw[:, k], m), ACT.Copy,
                                         scale=w_scale[:, 0:1]).then_inc(s_whi, 1)

            def bring_table(before):
                if before is not None:
                    act.wait_ge(s_table, before)
                nc.scalar.activation(table[:, :], ones[0:1, 0:1], ACT.Sigmoid).then_inc(s_table, 1)

            act.wait_ge(s_ones, 1)
            bring_table(None)
            for k in range(BLOCKS):
                act.wait_ge(s_wx[k], 16)
                for m in range(BLOCKS):
                    nc.scalar.activation(packed(wx_hi[:, k, m]), by_block(wx_raw[:, k], m), ACT.Copy).then_inc(s_wxhi, 1)
                if k == 0:
                    act.wait_ge(s_scale, 5)
                cut_x(0, 0, k)
                cut_wh(k)
            unscale = act.alloc_register("unscale")
            act.wait_ge(s_scale, 6)
            act.reg_load(unscale, un_scale[0:1, 0:1].bitcast(I32))

            def step(turn, s):
                t, slot, col = turn * ACT_STEPS + s, s % ROUND // CHUNK, s % CHUNK
                psum = gates[slot]
                act.wait_ge(s_pg, t + 1)
                g0 = REGIONS[GATE_G, 0]
                nc.scalar.activation(gc[:, :, 0, :], psum[:, g0:g0 + 2, col, :], ACT.Tanh, scale=unscale).then_inc(s_tanh_g, 1)
                for m in range(BLOCKS):
                    act.wait_ge(s_pif[m], t + 1)
                    i = REGIONS[GATE_I, m]
                    nc.scalar.activation(sig_if[:, m], psum[:, i:i + 2, col, :], ACT.Sigmoid, scale=unscale).then_inc(s_sig_if[m], 1)
                act.wait_ge(s_po, t + 1)
                o0 = REGIONS[GATE_O, 0]
                nc.scalar.activation(sig_o[:, :].rearrange("p (m b) -> p m b", b=B), psum[:, o0:o0 + 2, col, :],
                                     ACT.Sigmoid, scale=unscale).then_inc(s_sig_o, 1)
                for m in range(BLOCKS):
                    act.wait_ge(s_c[m], t + 1)
                    nc.scalar.activation(tanh_c[:, quad(m)], gc[:, m, 1, :], ACT.Tanh).then_inc(s_tanh_c[m], 1)

            def steps(turn, count, last=False):
                bring_table(turn + 1)
                for s in range(count):
                    step(turn, s)
                    if s % CHUNK < BLOCKS and not (last and s >= count - CHUNK):
                        cut_x(1 - s % ROUND // CHUNK, turn * (ACT_STEPS // CHUNK) + s // CHUNK + 1, s % CHUNK)

            with act.Fori(0, T // ACT_STEPS - 1) as turn:
                steps(turn, ACT_STEPS)
            steps(T // ACT_STEPS - 1, ACT_STEPS, last=True)
            act.wait_ge(s_y, (T // CHUNK - 1) * 2 + len(LAST_PIECES))
            store_step(act, CHUNK - 1)

        @block.tensor
        def _(pe):
            def add_bias(slot, g, m, start=False):
                nc.tensor.matmul(gates[slot][:, REGIONS[g, m]], bias_parts[:, m, g],
                                 ones[:, :].rearrange("p (s b) -> p s b", b=B),
                                 start=start, stop=False, skip_group_check=True)

            def project(slot, kind, g, m, k, start=False):
                weights, inputs = {"hi": (wx_hi, xT_hi), "cross": (wx_lo, xT_hi), "lo": (wx_hi, xT_lo)}[kind]
                nc.tensor.matmul(gates[slot][:, REGIONS[g, m]], weights[:, k, m, g], inputs[:, k],
                                 start=start, stop=False, skip_group_check=True)

            PRODUCTS = [(kind, g, m, k) for k in range(BLOCKS) for kind in ("hi", "cross")
                        for g in range(GATES) for m in range(BLOCKS)]
            PRODUCTS += [("lo", g, m, k) for k in range(BLOCKS) for g in range(GATES) for m in range(BLOCKS)]
            STEP_WORK = -(-len(PRODUCTS) // (CHUNK - 1))

            def chunk_work(slot, chunk, col):
                if col == 0:
                    for (g, m), region in REGIONS.items():
                        add_bias(slot, g, m, start=(region % 2 == 0))
                    return
                for kind, g, m, k in PRODUCTS[STEP_WORK * (col - 1):STEP_WORK * col]:
                    if g == 0 and m == 0 and kind != "cross":
                        pe.wait_ge(s_xhi if kind == "hi" else s_xlo, chunk * BLOCKS + k + 1)
                    project(slot, kind, g, m, k)

            def accumulate(slot, col, g, m, k, weights, state):
                return nc.tensor.matmul(gates[slot][:, REGIONS[g, m], col], weights[:, k, m, g], state[:, quad(k)],
                                        start=False, stop=False, skip_group_check=True)

            def leading(slot, col, k, which):
                for g, m in which:
                    accumulate(slot, col, g, m, k, wh_hi, h_hi)
                    accumulate(slot, col, g, m, k, wh_lo, h_hi)

            def rest(slot, col, k, which):
                for g, m in which:
                    done = accumulate(slot, col, g, m, k, wh_hi, h_lo)
                return done

            G = [(GATE_G, 0), (GATE_G, 1)]
            IF0 = [(GATE_I, 0), (GATE_F, 0)]
            IF1 = [(GATE_I, 1), (GATE_F, 1)]
            O = [(GATE_O, 0), (GATE_O, 1)]

            def step(turn, s, last=False):
                t, slot, col = turn * ROUND + s, s // CHUNK, s % CHUNK
                pe.wait_ge(s_hi[0], t)
                leading(slot, col, 0, G + IF0 + IF1)
                pe.wait_ge(s_hi[1], t)
                leading(slot, col, 1, G + IF0)
                pe.wait_ge(s_lo[0], t)
                rest(slot, col, 0, G + IF0)
                pe.wait_ge(s_lo[1], t)
                rest(slot, col, 1, G).then_inc(s_pg, 1)
                rest(slot, col, 1, IF0).then_inc(s_pif[0], 1)
                leading(slot, col, 1, IF1)
                rest(slot, col, 0, IF1)
                rest(slot, col, 1, IF1).then_inc(s_pif[1], 1)
                for k in range(BLOCKS):
                    leading(slot, col, k, O)
                    done = rest(slot, col, k, O)
                done.then_inc(s_po, 1)
                if not (last and slot == SLOTS - 1):
                    chunk_work(1 - slot, turn * SLOTS + slot + 1, col)

            pe.wait_ge(s_ones, 1)
            pe.wait_ge(s_wh[0], 16)
            for _ in range(WARM_UP):
                nc.tensor.matmul(gates[0][:, 0], ones[:, 0:P], ones[:, :].rearrange("p (s b) -> p s b", b=B),
                                 start=True, stop=True, skip_group_check=True)

            def first_products(which):
                for kind, k in (("hi", 0), ("cross", 0), ("lo", 0), ("hi", 1), ("lo", 1), ("bias", 0), ("cross", 1)):
                    if kind in ("hi", "lo"):
                        pe.wait_ge(s_xhi if kind == "hi" else s_xlo, k + 1)
                    elif kind == "bias":
                        pe.wait_ge(s_bparts, 16 * PARTS)
                    for m in range(BLOCKS):
                        if kind == "cross":
                            pe.wait_ge(s_wxlo[k], m + 1)
                        elif kind == "hi":
                            pe.wait_ge(s_wxhi, k * BLOCKS + m + 1)
                        for g in which:
                            if kind == "bias":
                                add_bias(0, g, m)
                            else:
                                opens = kind == "hi" and k == 0 and (g == GATE_I or (m == 0 and g in (GATE_G, GATE_O)))
                                project(0, kind, g, m, k, start=opens)

            def first_step(which, done):
                for g, m in which:
                    for k in range(BLOCKS):
                        for part in range(PARTS):
                            accumulate(0, 0, g, m, k, wh_hi, cond_parts[:, part])
                            end = accumulate(0, 0, g, m, k, wh_lo, cond_parts[:, part])
                end.then_inc(done, 1)

            first_products((GATE_G, GATE_I, GATE_F))
            pe.wait_ge(s_cparts, PARTS)
            pe.wait_ge(s_whi, BLOCKS * BLOCKS)
            pe.wait_ge(s_wlo, BLOCKS * BLOCKS)
            for which, done in ((G, s_pg), (IF0, s_pif[0]), (IF1, s_pif[1])):
                first_step(which, done)
            first_products((GATE_O,))
            first_step(O, s_po)
            chunk_work(1, 1, 0)
            for s in range(1, ROUND):
                step(0, s)
            with pe.Fori(1, ROUNDS - 1) as turn:
                for s in range(ROUND):
                    step(turn, s)
            for s in range(ROUND):
                step(ROUNDS - 1, s, last=True)

        @block.vector
        def _(dve):
            def transpose_x(slot, k):
                nc.vector.transpose(xT[:, slot, :, k, :], x_sb[:, slot, :, quad(k)]).then_inc(s_xT, 1)

            def rest_x(slot, chunk, k):
                dve.wait_ge(s_xhi, chunk * BLOCKS + k + 1)
                nc.vector.scalar_tensor_tensor(xT_lo[:, k], xT[:, slot, :, k, :], full_scale[:, 0:1],
                                               xT_hi[:, k].bitcast(F32), ALU.mult, ALU.subtract).then_inc(s_xlo, 1)

            def residual(t, s):
                slot, col = s // CHUNK, s % CHUNK
                dve.wait_ge(s_h[1], t + 1)
                nc.vector.scalar_tensor_tensor(yT[:, slot, col], h_f32[:, :], 1.0 / H_SCALE,
                                               xT[:, slot, col].rearrange("p k b -> p (k b)"),
                                               ALU.mult, ALU.add).then_inc(s_yT, 1)

            def transpose_y(slot, cols):
                steps = slice(cols.start, cols.stop)
                nc.vector.transpose(y_sb[:, slot, steps].rearrange("p t c -> p (t c)"),
                                    yT[:, slot, steps].rearrange("p t c -> p (t c)")).then_inc(s_y, 1)

            def wait_stored(turn, slot):
                if isinstance(turn, int) and turn == 0:
                    return
                dve.wait_ge(s_stored[slot], turn * DMA)

            def background(turn, s, first, last):
                t, slot, col = turn * ROUND + s, s // CHUNK % SLOTS, s % CHUNK
                chunk = turn * SLOTS + s // CHUNK
                if not (last and slot == SLOTS - 1):
                    if col < BLOCKS:
                        if col == 0 and first and s == 0:
                            dve.wait_ge(s_x[1], DMA)
                        elif col == 0:
                            dve.wait_ge(s_yT, t)
                        transpose_x(1 - slot, col)
                    elif col < 2 * BLOCKS:
                        rest_x(1 - slot, chunk + 1, col - BLOCKS)
                if 4 <= col < 6 and not (first and slot == 0):
                    if col == 4:
                        wait_stored(turn + (s // CHUNK - 1) // SLOTS, 1 - slot)
                    transpose_y(1 - slot, HALVES[col - 4])
                if last and s >= ROUND - 2:
                    if s == ROUND - 2:
                        wait_stored(turn, slot)
                    transpose_y(slot, LAST_PIECES[s - ROUND + 2])

            def step(turn, s, first=False, last=False):
                t = turn * ROUND + s
                if s % CHUNK == CHUNK - 1 and not last:
                    dve.wait_ge(s_x[s // CHUNK % SLOTS], (turn + s // ROUND + 2) * DMA)
                if not (first and s == 0):
                    residual(t - 1, (s - 1) % ROUND)
                background(turn, s, first, last)
                for m in range(BLOCKS):
                    dve.wait_ge(s_sig_if[m], t + 1)
                    nc.vector.tensor_tensor(prod[:, m], sig_if[:, m], gc[:, m], ALU.mult).then_inc(s_prod[m], 1)
                for m in range(BLOCKS):
                    dve.wait_ge(s_prod[m], t + 1)
                    nc.vector.tensor_tensor(gc[:, m, 1], prod[:, m, 0], prod[:, m, 1], ALU.add).then_inc(s_c[m], 1)
                for m in range(BLOCKS):
                    dve.wait_ge(s_tanh_c[m], t + 1)
                    for dst, done in ((h_hi, s_hi), (h_f32, s_h)):
                        nc.vector.scalar_tensor_tensor(dst[:, quad(m)], sig_o[:, quad(m)], H_SCALE, tanh_c[:, quad(m)],
                                                       ALU.mult, ALU.mult).then_inc(done[m], 1)
                for m in range(BLOCKS):
                    dve.wait_ge(s_h[m], t + 1)
                    nc.vector.tensor_tensor(h_lo[:, quad(m)], h_f32[:, quad(m)], h_hi[:, quad(m)],
                                            ALU.subtract).then_inc(s_lo[m], 1)

            nc.vector.memset(ones[:, :], 1.0).then_inc(s_ones, 1)
            nc.vector.memset(gc[:, :, :, :], 0.0).then_inc(s_czero, 1)
            for k in range(BLOCKS):
                dve.wait_ge(s_wh[k], 16)
                nc.vector.tensor_reduce(w_max_of[:, k:k + 1], wh_raw[:, k], AX_X, ALU.max,
                                        apply_absolute_value=True).then_inc(s_wmax, 1)
            dve.wait_ge(s_wmax, BLOCKS)
            nc.vector.tensor_tensor(w_max[:, :], w_max_of[:, 0:1], w_max_of[:, 1:2], ALU.max).then_inc(s_wmax, 1)
            dve.wait_ge(s_cond, 16)
            nc.vector.transpose(cond_T[:, :], cond_sb[:, :]).then_inc(s_cstep, 1)
            dve.wait_ge(s_all_max, 1)
            nc.vector.tensor_scalar(w_clamped[:, :], w_all_max[:, :], W_LEAST, None, ALU.max).then_inc(s_scale, 1)
            dve.wait_ge(s_scale, 1)
            nc.vector.tensor_scalar(w_pow2[:, :].bitcast(I32), w_clamped[:, :].bitcast(I32), EXPONENT, None,
                                    ALU.bitwise_and).then_inc(s_scale, 1)
            dve.wait_ge(s_scale, 2)
            nc.vector.reciprocal(w_inv[:, :], w_pow2[:, :]).then_inc(s_scale, 1)
            dve.wait_ge(s_scale, 3)
            nc.vector.tensor_scalar(full_scale[:, :], w_inv[:, :], W_TOP * H_SCALE, None, ALU.mult).then_inc(s_scale, 1)
            nc.vector.tensor_scalar(w_scale[:, :], w_inv[:, :], W_TOP, None, ALU.mult).then_inc(s_scale, 1)
            nc.vector.tensor_scalar(un_scale[:, :], w_pow2[:, :], 1.0 / (W_TOP * H_SCALE), None, ALU.mult).then_inc(s_scale, 1)
            dve.wait_ge(s_x[0], DMA)
            for k in range(BLOCKS):
                transpose_x(0, k)

            def rest_wh(k, m):
                dve.wait_ge(s_whi, k * BLOCKS + m + 1)
                nc.vector.scalar_tensor_tensor(packed(wh_lo[:, k, m]), by_block(wh_raw[:, k], m), w_scale[:, 0:1],
                                               packed(wh_hi[:, k, m]), ALU.mult, ALU.subtract).then_inc(s_wlo, 1)

            dve.wait_ge(s_scale, 6)
            for m in range(BLOCKS):
                dve.wait_ge(s_wxhi, m + 1)
                rest_wx(nc.vector, 0, m)
            for k in range(BLOCKS):
                rest_x(0, 0, k)
                for m in range(BLOCKS):
                    rest_wh(k, m)

            dve.wait_ge(s_czero, 1)
            for s in range(ROUND):
                step(0, s, first=True)
            for s in range(DVE_TURN):
                step(1, s)
            with dve.Fori(1, ROUNDS - 1) as turn:
                for s in range(DVE_TURN, ROUND + DVE_TURN):
                    step(turn, s)
            for s in range(DVE_TURN, ROUND):
                step(ROUNDS - 1, s, last=True)
            residual(T - 1, ROUND - 1)
            dve.wait_ge(s_yT, T)
            transpose_y(SLOTS - 1, LAST_PIECES[-1])


_INS = ["x", "cond_1024", "L0_cond_Wx", "L0_cond_Wh", "L0_cond_b"]


def kernel(**inputs):
    import numpy as _np
    import concourse.bacc as _bacc
    from concourse import mybir as _mybir
    from concourse.bass_utils import run_bass_kernel_spmd as _run

    nc = _bacc.Bacc("TRN2", target_bir_lowering=False, num_devices=1)
    arrays, args = {}, []
    for name in _INS:
        a = _np.ascontiguousarray(inputs[name])
        arrays[f"in_{name}"] = a
        args.append(nc.dram_tensor(f"in_{name}", a.shape, _mybir.dt.from_np(a.dtype), kind="ExternalInput").ap())
    shape = arrays["in_x"].shape
    args.append(nc.dram_tensor("out_y", shape, _mybir.dt.from_np(arrays["in_x"].dtype), kind="ExternalOutput").ap())
    lstm_residual(nc, *args)
    r = _run(nc, [arrays], core_ids=[0])
    return r.results[0]["out_y"]
```
